# Optimizing a Trainium2 kernel written in Bass

```python
import numpy as np
import jax
import jax.numpy as jnp

def _softmax(x, axis=-1):
    return jax.nn.softmax(x, axis=axis)
def _gelu(x):
    return jax.nn.gelu(x, approximate=True)
def _silu(x):
    return jax.nn.silu(x)
def _sigmoid(x):
    return jax.nn.sigmoid(x)
def _layernorm(x, axis=-1, eps=1e-5):
    m = jnp.mean(x, axis=axis, keepdims=True)
    v = jnp.var(x, axis=axis, keepdims=True)
    return (x - m) / jnp.sqrt(v + eps)
def _scatter_add(tgt, idx, src, axis=0):
    return tgt.at[idx].add(src)
def _segment_sum(src, seg, n):
    return jax.ops.segment_sum(src, seg, n)

kernel_name = 'mk_conv_preact_d1_conv_nchw256_efd0a5'

def setup_inputs(seed: int = 0):
    np.random.seed(seed)
    _w = jnp.asarray
    def _rec_inputs():
        import jax
        import jax.numpy as jnp
        _gk = jax.random.key(seed)
        x = -0.0003957 + 1 * jax.random.normal(jax.random.fold_in(_gk, 1), (16, 256, 56, 56), jnp.float32)
        return x
    x = _rec_inputs()
    def _L0_conv_setup():
        import jax, jax.numpy as jnp
        import numpy as np
        OFFSETS8 = ((0, 1), (0, -1), (1, 0), (-1, 0), (1, 1), (1, -1), (-1, 1), (-1, -1))
        DIRS = 8
        key = jax.random.key(seed)
        k1, k2, k3, k4 = jax.random.split(key, 4)
        B, C, H, W = (16, 256, 56, 56)
        x = jax.random.normal(k1, (B, C, H, W), dtype=jnp.float32)
        dw_weight = jax.random.normal(k2, (C, 1, 3, 3), dtype=jnp.float32) * 0.1
        pw_weight = jax.random.normal(k3, (DIRS * C, C), dtype=jnp.float32) * 0.05
        pw_bias = jax.random.normal(k4, (DIRS * C,), dtype=jnp.float32) * 0.01
        return {'x': x, 'dw_weight': dw_weight, 'pw_weight': pw_weight, 'pw_bias': pw_bias}
    _L0_conv_all = _L0_conv_setup()
    _L0_conv_in = {k: v for k, v in _L0_conv_all.items() if k in ('dw_weight', 'pw_weight', 'pw_bias', )}
    del _L0_conv_all

    return {
        "x": x,
        "L0_conv_dw_weight": _L0_conv_in["dw_weight"],
        "L0_conv_pw_weight": _L0_conv_in["pw_weight"],
        "L0_conv_pw_bias": _L0_conv_in["pw_bias"],
    }

def reference(x, L0_conv_dw_weight, L0_conv_pw_weight, L0_conv_pw_bias):
    import jax
    import jax.numpy as jnp
    def _L0_conv_ref(x, dw_weight, pw_weight, pw_bias):
        import jax, jax.numpy as jnp
        import numpy as np
        OFFSETS8 = ((0, 1), (0, -1), (1, 0), (-1, 0), (1, 1), (1, -1), (-1, 1), (-1, -1))
        DIRS = 8
        B, C, H, W = x.shape
        h = jax.lax.conv_general_dilated(x, dw_weight, window_strides=(1, 1), padding=((1, 1), (1, 1)), dimension_numbers=('NCHW', 'OIHW', 'NCHW'), feature_group_count=C)
        h = jax.nn.gelu(h, approximate=False)
        maps = jnp.einsum('bchw,oc->bohw', h, pw_weight) + pw_bias[None, :, None, None]
        maps = maps.reshape(B, DIRS, C, H, W)
        out = jnp.zeros_like(x)
        for i, (dx, dy) in enumerate(OFFSETS8):
            diff = jnp.roll(x, shift=(dy, dx), axis=(-2, -1)) - x
            out = out + maps[:, i] * diff
        return out

    def _gn(v, G=32, eps=1e-5):
        B_, C_, H_, W_ = v.shape
        g = v.reshape(B_, G, C_ // G, H_, W_)
        m = jnp.mean(g, axis=(2, 3, 4), keepdims=True)
        s = jnp.var(g, axis=(2, 3, 4), keepdims=True)
        return ((g - m) / jnp.sqrt(s + eps)).reshape(v.shape)

    def _ln_c(v, eps=1e-6):
        m = jnp.mean(v, axis=1, keepdims=True)
        s = jnp.var(v, axis=1, keepdims=True)
        return (v - m) / jnp.sqrt(s + eps)

    def _ln_t(v, eps=1e-5):
        m = jnp.mean(v, axis=-1, keepdims=True)
        s = jnp.var(v, axis=-1, keepdims=True)
        return (v - m) / jnp.sqrt(s + eps)

    def _to_tokens(v):
        B_, C_, H_, W_ = v.shape
        return v.reshape(B_, C_, H_ * W_).transpose(0, 2, 1)
    def _from_tokens(t, like):
        B_, C_, H_, W_ = like.shape
        return t.transpose(0, 2, 1).reshape(B_, C_, H_, W_)

    x = x + _L0_conv_ref(_gn(x), L0_conv_dw_weight, L0_conv_pw_weight, L0_conv_pw_bias)
    return x


_drawn_inputs = setup_inputs


def setup_inputs(seed=0):
    import zlib

    import numpy as np

    out = dict(_drawn_inputs(seed))
    spreads = {}
    factors = {}
    for name, (base, spread) in spreads.items():
        noise = np.random.default_rng([zlib.crc32(name.encode()), seed]).standard_normal(out[name].shape)
        drawn = base * np.exp(spread * noise) if base else spread * noise
        out[name] = jnp.asarray(drawn.astype(out[name].dtype))
    for name, factor in factors.items():
        out[name] = (out[name] * factor).astype(out[name].dtype)
    return out
```

```python
import concourse.bass as bass
from concourse import mybir
from contextlib import ExitStack


def preact_directional_conv(nc, x, pw_t, pw_b, dw, out):
    F32, F32R = mybir.dt.float32, mybir.dt.float32r
    ALU, ACT, AX = mybir.AluOpType, mybir.ActivationFunctionType, mybir.AxisListType

    P = 128
    B, C, H, W = x.shape
    HALVES = C // P
    DIRS = 8
    ROWS = 8
    TILES = H // ROWS
    PX = ROWS * W
    HP, WP = H + 2, W + 2
    TR = ROWS + 2
    PLANE = HP * WP
    GROUP = 8
    EPS = 1e-5
    STEPS = 2 * TILES
    BODIES = B // 2
    BANK = 512
    SLICES = 4
    SROWS = H // SLICES

    E3 = (ROWS + 1) * WP
    E1 = ROWS * WP
    PAIRS = ((0, 1, 1, WP), (2, 3, 3, 1), (4, 7, 0, WP + 1), (6, 5, 2, WP - 1))
    NP = len(PAIRS)

    TAPS_PE = ((0, 1), (0, 1, 2))
    TAPS_DVE = tuple(tuple(t for t in range(9) if t not in pe) for pe in TAPS_PE)
    ND = max(len(t) for t in TAPS_PE)

    def taps_before(n, g):
        return n * (len(TAPS_DVE[0]) + len(TAPS_DVE[1])) + sum(len(t) for t in TAPS_DVE[:g])

    SPARED = (0, 1)
    ADDS = tuple(NP - 1 - sp for sp in SPARED)
    ACCS = sum(ADDS)

    PAIRS_BODY = STEPS * HALVES * NP
    GROUPS = [q % 3 for q in range(PAIRS_BODY - 1)] + [1]

    def last_user(q):
        p = q - 1
        while GROUPS[p % PAIRS_BODY] != GROUPS[q]:
            p -= 1
        return p

    x_src = x.rearrange("b (g p) h w -> b g p h w", p=P)
    out_dst = out.rearrange("b (g p) h w -> b p g (h w)", p=P)

    ctx = ExitStack()
    with ctx:
        def sb(name, shape, dt=F32):
            return ctx.enter_context(nc.sbuf_tensor(name, shape, dt))

        def sem(name):
            return ctx.enter_context(nc.semaphore(name))

        def window(base, dims):
            return bass.AP(base.tensor, base.offset, [list(base.ap[0])] + [list(d) for d in dims])

        GUARD = 2
        xpad_t = [sb(f"xpad{i}", [P, GUARD + HALVES * PLANE]) for i in range(2)]
        xpad = [t[:, GUARD:].rearrange("p (g r c) -> p g r c", g=HALVES, c=WP) for t in xpad_t]
        xn = [sb(f"xn{i}", [P, HALVES, TR, WP]) for i in range(2)]
        xhi = [sb(f"xhi{i}", [P, HALVES, TR, WP], F32R) for i in range(2)]
        xlo = [sb(f"xlo{i}", [P, HALVES, TR, WP], F32R) for i in range(2)]
        hid = [sb(f"hid{i}", [P, HALVES, PX]) for i in range(2)]
        hhi = [sb(f"hhi{i}", [P, HALVES, PX], F32R) for i in range(2)]
        hlo = [sb(f"hlo{i}", [P, HALVES, PX], F32R) for i in range(2)]
        ediff = [[sb(f"ediff{i}{g}", [P, 3 * E3 + E1]) for g in range(HALVES)] for i in range(2)]
        acc = [sb(f"acc{i}", [P, HALVES, 2, PX]) for i in range(2)]
        spare = sb("spare", [P, 2, PX])
        outb = [sb(f"outb{i}", [P, HALVES, PX]) for i in range(2)]

        w_raw = xpad_t[1][:, 0:HALVES * DIRS * C].rearrange("p (k m) -> p k m", k=HALVES)
        w_hi = sb("w_hi", [P, HALVES, DIRS * C], F32R)
        w_lo = sb("w_lo", [P, HALVES, DIRS * C], F32R)
        dw_f = sb("dw_f", [P, HALVES, 9])
        dw_hi = sb("dw_hi", [P, HALVES, 9], F32R)
        dw_lo = sb("dw_lo", [P, HALVES, 9])
        diag_hi = sb("diag_hi", [P, HALVES, ND, P], F32R)
        diag_lo = sb("diag_lo", [P, HALVES, ND, P], F32R)
        ident = sb("ident", [P, P])
        pb_f = sb("pb_f", [P, HALVES, DIRS])
        zeros = sb("zeros", [P, HALVES, 1, WP])
        neg_half = sb("neg_half", [P, HALVES])

        squares_out = sb("squares_out", [P, SROWS, W])
        part_sums = sb("part_sums", [P, HALVES, SLICES])
        part_neg = sb("part_neg", [P, HALVES, SLICES])
        part_sq = sb("part_sq", [P, HALVES, SLICES])
        neg_mean_c = sb("neg_mean_c", [P, HALVES])
        moments = sb("moments", [P, 32])
        mom_t = sb("mom_t", [P, 32])
        sums = sb("sums", [P, 4])
        mean_t = sb("mean_t", [P, 32])
        dev_t = sb("dev_t", [P, 32])
        devs_t = sb("devs_t", [P, 32])
        mean_b = sb("mean_b", [P, 32])
        devs_b = sb("devs_b", [P, 32])
        var_eps = sb("var_eps", [P, HALVES])
        neg_mean = sb("neg_mean", [P, HALVES])
        rstd = [sb(f"rstd{i}", [P, HALVES]) for i in range(2)]
        shift = [sb(f"shift{i}", [P, HALVES]) for i in range(2)]
        bias = [sb(f"bias{i}", [P, HALVES, DIRS]) for i in range(2)]

        psum = ctx.enter_context(nc.psum_tensor("psum", [P, 8, BANK], F32))

        def conv_bank(g):
            return psum[:, g, 0:PX]

        def maps(q):
            b = 2 + 2 * GROUPS[q % PAIRS_BODY]
            return psum[:, b:b + 2, 0:PX]

        weights_in = sem("weights_in")
        small_in = sem("small_in")
        x_in = [[sem(f"x_in{i}{g}") for g in range(HALVES)] for i in range(2)]
        out_sent = [sem(f"out_sent{i}") for i in range(2)]
        consts = sem("consts")
        split = sem("split")
        taps_split = sem("taps_split")
        measure = sem("measure")
        stat = sem("stat")
        scales = sem("scales")
        wraps = sem("wraps")
        xn_s = sem("xn_s")
        xhi_s = sem("xhi_s")
        xlo_s = sem("xlo_s")
        conv_s = sem("conv_s")
        tap_s = sem("tap_s")
        gelu_s = sem("gelu_s")
        hhi_s = sem("hhi_s")
        hlo_s = sem("hlo_s")
        ediff_s = sem("ediff_s")
        maps_s = sem("maps_s")
        biased_s = sem("biased_s")
        prod_s = sem("prod_s")
        acc_s = sem("acc_s")
        spare_s = sem("spare_s")
        fold_s = sem("fold_s")
        final_s = sem("final_s")
        PROD0, ACC0, SPARE0, FOLD0, FINAL0, SENT0 = 2 * NP, ACCS, 1, 2, 1, 16
        MEASURES = 2 * HALVES * SLICES + HALVES
        STAT = 14
        CONSTS = 8

        assert sum(SPARED) <= 1

        def added(n0, nl, g):
            return n0 * ACCS + (nl * ACCS + sum(ADDS[:g]) + ACC0)

        block = ctx.enter_context(nc.Block())

        def loop(engine, body):
            with engine.Fori(0, BODIES - 1) as i:
                body(i * STEPS, i * 2, False)
            body((BODIES - 1) * STEPS, (BODIES - 1) * 2, True)

        @block.sync
        def _(sp):
            def load_image(b, par):
                for g in range(HALVES):
                    sp.dma_start(xpad[par][:, g, 1:H + 1, 1:W + 1], x_src[b, g]).then_inc(x_in[par][g], 16)

            load_image(0, 0)
            for par in range(2):
                sp.sem_inc(out_sent[par], SENT0)
            sp.dma_start(dw_f[:], dw.rearrange("(g p) t -> p g t", p=P)).then_inc(small_in, 16)
            sp.dma_start(pb_f[:], pw_b).then_inc(small_in, 16)
            sp.dma_start(w_raw, pw_t.rearrange("(k p) m -> p k m", p=P)).then_inc(weights_in, 16)
            sp.wait_ge(split, 2)

            def body(n0, b0, last):
                for nl in range(STEPS):
                    t, par = nl % TILES, (nl // TILES) % 2
                    if t == 0 and not (last and nl):
                        sp.wait_ge(final_s, n0 + (nl + FINAL0))
                        load_image(b0 + par + 1, 1 - par)
                    sp.wait_ge(final_s, n0 + (nl + 1 + FINAL0))
                    sp.dma_start(out_dst[b0 + par, :, :, t * PX:(t + 1) * PX],
                                 outb[nl % 2][:]).then_inc(out_sent[nl % 2], 16)

            loop(sp, body)
            for par in range(2):
                sp.wait_ge(out_sent[par], 16 * B * TILES // 2 + SENT0)

        @block.gpsimd
        def _(pool):
            nc.gpsimd.memset(ident[:], 0.0).then_inc(consts, 1)
            pool.wait_ge(consts, 1)
            nc.gpsimd.affine_select(out=ident[:], in_=ident[:], compare_op=ALU.not_equal, fill=1.0, base=0,
                                    pattern=[[-1, P]], channel_multiplier=1).then_inc(consts, 1)
            nc.gpsimd.memset(neg_half[:], -0.5).then_inc(consts, 1)
            nc.gpsimd.memset(zeros[:], 0.0).then_inc(consts, 1)
            nc.gpsimd.memset(moments[:], 0.0).then_inc(consts, 1)
            nc.gpsimd.memset(xpad_t[0][:, 0:GUARD], 0.0).then_inc(consts, 1)
            for par in range(2):
                nc.gpsimd.memset(xn[par][:], 0.0).then_inc(consts, 1)
            pool.sem_inc(final_s, FINAL0)
            pool.sem_inc(fold_s, FOLD0)
            pool.sem_inc(spare_s, SPARE0)

            def norm_scales(j, par):
                pool.wait_ge(stat, j * STAT + STAT)
                nc.gpsimd.tensor_tensor(rstd[par][:], var_eps[:], neg_half[:], ALU.pow).then_inc(scales, 1)
                pool.wait_ge(scales, j * 3 + 1)
                nc.gpsimd.tensor_tensor(shift[par][:], neg_mean[:], rstd[par][:], ALU.mult).then_inc(scales, 1)
                nc.gpsimd.tensor_tensor(bias[par][:], pb_f[:], window(rstd[par][:], [[1, HALVES], [0, DIRS]]),
                                        ALU.mult).then_inc(scales, 1)

            def split_x(n, nl):
                par = nl % 2
                pool.wait_ge(xhi_s, n + 1)
                nc.gpsimd.tensor_tensor(xlo[par][:], xn[par][:], xhi[par][:].bitcast(F32),
                                        ALU.subtract).then_inc(xlo_s, 1)

            def split_h(n, nl):
                par = nl % 2
                pool.wait_ge(hhi_s, n + 1)
                nc.gpsimd.tensor_tensor(hlo[par][:], hid[par][:], hhi[par][:].bitcast(F32),
                                        ALU.subtract).then_inc(hlo_s, 1)

            def differences(n, nl, b, g):
                t, par = nl % TILES, (nl // TILES) % 2
                top = GUARD + g * PLANE + t * ROWS * WP
                above = xpad_t[par][:, top - 1:top]
                center = xpad_t[par][:, top + WP:top + WP + 1]
                left = xpad_t[par][:, top + WP - 1:top + WP]
                if t == 0 and g == 0:
                    pool.wait_ge(wraps, b * 4 + 4)
                if nl > 1 or not isinstance(n, int):
                    pool.wait_ge(prod_s, n * 2 * NP + ((g + 1 - 4) * NP + PROD0))
                nc.gpsimd.tensor_tensor(
                    window(ediff[nl % 2][g][:, 0:1], [[E3, 3], [1, E3]]), window(above, [[1, 3], [1, E3]]),
                    window(center, [[0, 3], [1, E3]]), ALU.subtract).then_inc(ediff_s, 1)
                nc.gpsimd.tensor_tensor(
                    ediff[nl % 2][g][:, 3 * E3:], window(left, [[1, E1]]), window(center, [[1, E1]]),
                    ALU.subtract).then_inc(ediff_s, 1)

            def finish(n, nl):
                t, par, ip = nl % TILES, nl % 2, (nl // TILES) % 2
                a, o = acc[par], outb[par]
                for g in range(HALVES):
                    if SPARED[g]:
                        pool.wait_ge(prod_s, n * 2 * NP + ((g + 1) * NP + PROD0))
                        pool.wait_ge(acc_s, added(n, 0, g) + ADDS[g])
                        nc.gpsimd.tensor_tensor(a[:, g], a[:, g], spare[:], ALU.add).then_inc(spare_s, 1)
                pool.wait_ge(acc_s, added(n, 1, 0))
                if any(SPARED):
                    pool.wait_ge(spare_s, n + (1 + SPARE0))
                pool.wait_ge(out_sent[par], (n - nl) * 8 + (16 * (nl // 2) + SENT0))
                nc.gpsimd.tensor_tensor(o[:], a[:, :, 0, :], a[:, :, 1, :], ALU.subtract).then_inc(fold_s, 1)
                pool.wait_ge(fold_s, n + (1 + FOLD0))
                o = o[:].rearrange("p g (r c) -> p g r c", c=W)
                nc.gpsimd.tensor_tensor(o, o, xpad[ip][:, :, t * ROWS + 1:(t + 1) * ROWS + 1, 1:W + 1],
                                        ALU.add).then_inc(final_s, 1)

            pool.wait_ge(consts, CONSTS)
            pool.wait_ge(small_in, 32)
            norm_scales(0, 0)
            split_x(0, 0)
            split_x(1, 1)
            differences(0, 0, 0, 0)
            differences(0, 0, 0, 1)
            pool.wait_ge(split, 2)
            nc.gpsimd.memset(xpad_t[1][:, 0:GUARD], 0.0).then_inc(consts, 1)
            pool.wait_ge(consts, CONSTS + 1)
            split_h(0, 0)
            split_x(2, 2)

            def slot(n, nl, b0, last):
                t, b = nl % TILES, b0 + nl // TILES
                more = lambda k: not (last and nl + k >= STEPS)
                if nl:
                    finish(n - 1, nl - 1)
                if more(1):
                    differences(n + 1, nl + 1, b0 + (nl + 1) // TILES, 0)
                if more(3):
                    split_x(n + 3, nl + 3)
                if more(1):
                    split_h(n + 1, nl + 1)
                    differences(n + 1, nl + 1, b0 + (nl + 1) // TILES, 1)
                if t == 3 and more(TILES):
                    norm_scales(b + 1, 1 - (nl // TILES) % 2)

            slot(0, 0, 0, False)

            def body(n0, b0, last):
                for nl in range(1, STEPS + (not last)):
                    slot(n0 + nl, nl, b0, last)
                if last:
                    finish(n0 + STEPS - 1, STEPS - 1)

            loop(pool, body)

        @block.scalar
        def _(act):
            def wrap(b, par):
                for g in range(HALVES):
                    act.wait_ge(x_in[par][g], (b - par) * 8 + 16)
                v = xpad[par]
                nc.scalar.copy(v[:, :, 1:H + 1, 0:1], v[:, :, 1:H + 1, W:W + 1]).then_inc(wraps, 1)
                nc.scalar.copy(v[:, :, 1:H + 1, W + 1:WP], v[:, :, 1:H + 1, 1:2]).then_inc(wraps, 1)
                act.wait_ge(wraps, b * 4 + 2)
                nc.scalar.copy(v[:, :, 0:1, :], v[:, :, H:H + 1, :]).then_inc(wraps, 1)
                nc.scalar.copy(v[:, :, H + 1:HP, :], v[:, :, 1:2, :]).then_inc(wraps, 1)

            def rows_of(par, g, c):
                return xpad[par][:, g, 1 + c * SROWS:1 + (c + 1) * SROWS, 1:W + 1]

            def measure_step(b, par, i):
                g, j = divmod(i, 2 * SLICES + 1)
                if j == 0:
                    act.wait_ge(x_in[par][g], (b - par) * 8 + 16)
                if i:
                    act.wait_ge(measure, b * MEASURES + i)
                elif not isinstance(b, int) or b:
                    act.wait_ge(stat, b * STAT)
                if j < SLICES:
                    nc.scalar.activation(squares_out[:], rows_of(par, g, j), ACT.Copy,
                                         accum_out=part_sums[:, g, j:j + 1]).then_inc(measure, 1)
                elif j == SLICES:
                    nc.scalar.activation(part_neg[:, g, :], part_sums[:, g, :], ACT.Copy, scale=-1.0 / (H * W),
                                         accum_out=neg_mean_c[:, g:g + 1]).then_inc(measure, 1)
                else:
                    j -= SLICES + 1
                    nc.scalar.activation(squares_out[:], rows_of(par, g, j), ACT.Square,
                                         bias=neg_mean_c[:, g:g + 1],
                                         accum_out=part_sq[:, g, j:j + 1]).then_inc(measure, 1)

            def normalise(nl, b):
                t, par, ip = nl % TILES, nl % 2, (nl // TILES) % 2
                r0, r1 = (1 if t == 0 else 0), (TR - 1 if t == TILES - 1 else TR)
                if t == 0:
                    nc.scalar.copy(xn[par][:, :, 0:1, :], zeros[:]).then_inc(xn_s, 1)
                    act.wait_ge(scales, b * 3 + 3)
                if t == TILES - 1:
                    nc.scalar.copy(xn[par][:, :, TR - 1:TR, :], zeros[:]).then_inc(xn_s, 1)
                for g in range(HALVES):
                    nc.scalar.activation(
                        xn[par][:, g, r0:r1, 1:W + 1], xpad[ip][:, g, t * ROWS + r0:t * ROWS + r1, 1:W + 1],
                        ACT.Identity, bias=shift[ip][:, g:g + 1], scale=rstd[ip][:, g:g + 1]).then_inc(xn_s, 1)

            def split_x_hi(nl, b):
                t, par = nl % TILES, nl % 2
                act.wait_ge(xn_s, b * (2 * TILES + 2) + (2 * (t + 1) + 1 + (t == TILES - 1)))
                nc.scalar.copy(xhi[par][:], xn[par][:]).then_inc(xhi_s, 1)

            def gelu(n, nl, g):
                act.wait_ge(tap_s, taps_before(n, g + 1))
                nc.scalar.activation(hid[nl % 2][:, g, :], conv_bank(g), ACT.Gelu).then_inc(gelu_s, 1)

            def split_h_hi(n, nl):
                act.wait_ge(gelu_s, n * 2 + 2)
                nc.scalar.copy(hhi[nl % 2][:], hid[nl % 2][:]).then_inc(hhi_s, 1)

            def add_bias(n0, q, k):
                ip, g = (q // (2 * NP * TILES)) % 2, (q // NP) % 2
                for side in range(2):
                    d = PAIRS[k][side]
                    act.wait_ge(maps_s, n0 * (4 * NP) + (2 * q + side + 1))
                    m = maps(q)[:, side, :]
                    nc.scalar.activation(m, m, ACT.Identity, bias=bias[ip][:, g, d:d + 1],
                                         scale=rstd[ip][:, g:g + 1]).then_inc(biased_s, 1)

            MEASURE_AT = [(t, g, k) for t in (1, 2, 3) for g in range(HALVES) for k in range(NP)]
            MEASURE_AT = MEASURE_AT[:MEASURES]
            for i in range(MEASURES):
                measure_step(0, 0, i)
            wrap(0, 0)
            act.wait_ge(consts, CONSTS)
            normalise(0, 0)
            split_x_hi(0, 0)
            normalise(1, 0)
            split_x_hi(1, 0)
            gelu(0, 0, 0)
            gelu(0, 0, 1)
            split_h_hi(0, 0)
            normalise(2, 0)
            split_x_hi(2, 0)
            gelu(1, 1, 0)

            def body(n0, b0, last):
                for nl in range(STEPS):
                    t, par, n = nl % TILES, nl // TILES, n0 + nl
                    more = lambda k: not (last and nl + k >= STEPS)
                    b3 = b0 + (nl + 3) // TILES
                    q = nl * 2 * NP
                    def beside(g, k):
                        if (t, g, k) in MEASURE_AT and not (last and par):
                            measure_step(b0 + par + 1, 1 - par, MEASURE_AT.index((t, g, k)))

                    add_bias(n0, q, 0)
                    beside(0, 0)
                    add_bias(n0, q + 1, 1)
                    beside(0, 1)
                    if more(1):
                        gelu(n + 1, nl + 1, 1)
                    add_bias(n0, q + 2, 2)
                    beside(0, 2)
                    if more(3):
                        normalise(nl + 3, b3)
                    add_bias(n0, q + 3, 3)
                    beside(0, 3)
                    if more(3):
                        split_x_hi(nl + 3, b3)
                    add_bias(n0, q + 4, 0)
                    beside(1, 0)
                    if more(1):
                        split_h_hi(n + 1, nl + 1)
                    add_bias(n0, q + 5, 1)
                    beside(1, 1)
                    if more(2):
                        gelu(n + 2, nl + 2, 0)
                    add_bias(n0, q + 6, 2)
                    beside(1, 2)
                    if t == 2 and not (last and par):
                        wrap(b0 + par + 1, 1 - par)
                    add_bias(n0, q + 7, 3)
                    beside(1, 3)

            loop(act, body)

        @block.vector
        def _(dve):
            def group_stats(b):
                done = [0]

                def then(ins):
                    ins.then_inc(stat, 1)
                    done[0] += 1

                def wait():
                    dve.wait_ge(stat, b * STAT + done[0])

                by8 = lambda v: v.rearrange("p (a e) -> p a e", e=GROUP)
                wide = lambda v: window(v, [[1, 32 // GROUP], [0, GROUP]])
                dve.wait_ge(measure, b * MEASURES + MEASURES)
                then(nc.vector.reduce_sum(sums[:, 0:HALVES], part_sq[:], axis=AX.X))
                then(nc.vector.tensor_scalar(moments[:, 0:3:2], neg_mean_c[:], -1.0, None, ALU.mult))
                wait()
                then(nc.vector.tensor_scalar(moments[:, 1:4:2], sums[:, 0:HALVES], 1.0 / (H * W), None, ALU.mult))
                wait()
                then(nc.vector.transpose(mom_t[:], moments[:]))
                wait()
                then(nc.vector.reduce_sum(sums[:], by8(mom_t[:]), axis=AX.X))
                wait()
                then(nc.vector.tensor_scalar(by8(mean_t[:]), wide(sums[:]), 1.0 / GROUP, None, ALU.mult))
                wait()
                then(nc.vector.tensor_tensor(dev_t[:], mom_t[:], mean_t[:], ALU.subtract))
                wait()
                then(nc.vector.tensor_tensor(dev_t[:], dev_t[:], dev_t[:], ALU.mult))
                wait()
                then(nc.vector.reduce_sum(sums[:], by8(dev_t[:]), axis=AX.X))
                wait()
                then(nc.vector.tensor_scalar(by8(devs_t[:]), wide(sums[:]), 1.0 / GROUP, None, ALU.mult))
                wait()
                then(nc.vector.transpose(mean_b[:], mean_t[:]))
                then(nc.vector.transpose(devs_b[:], devs_t[:]))
                wait()
                then(nc.vector.scalar_tensor_tensor(var_eps[:], mean_b[:, 1:4:2], EPS, devs_b[:, 0:3:2],
                                                    ALU.add, ALU.add))
                then(nc.vector.tensor_scalar(neg_mean[:], mean_b[:, 0:3:2], -1.0, None, ALU.mult))

            def multiply(n0, q, k):
                nl, g = divmod(q // NP, 2)
                if k == 0:
                    dve.wait_ge(ediff_s, n0 * 4 + (4 * nl + 2 * g + 2))
                    if g == 0:
                        dve.wait_ge(fold_s, n0 + (nl - 1 + FOLD0))
                to = acc[nl % 2][:, g] if k == 0 else maps(q)
                if k == NP - 1 and SPARED[g]:
                    dve.wait_ge(spare_s, n0 + (nl + SPARE0))
                    to = spare[:]
                dve.wait_ge(biased_s, n0 * (4 * NP) + (2 * q + 2))
                _, _, e, step = PAIRS[k]
                diff = window(ediff[nl % 2][g][:, e * E3 + 1:e * E3 + 2], [[step, 2], [WP, ROWS], [1, W]])
                nc.vector.tensor_tensor(to.rearrange("p s (r c) -> p s r c", c=W),
                                        maps(q).rearrange("p s (r c) -> p s r c", c=W), diff,
                                        ALU.mult).then_inc(prod_s, 1)

            def accumulate(n0, q, k):
                nl, g = divmod(q // NP, 2)
                if k > ADDS[g]:
                    return
                dve.wait_ge(prod_s, n0 * (2 * NP) + (q + 1 + PROD0))
                if k > 1:
                    dve.wait_ge(acc_s, added(n0, nl, g) + (k - 1))
                a = acc[nl % 2][:, g]
                nc.vector.tensor_tensor(a, maps(q), a, ALU.add).then_inc(acc_s, 1)

            def tap(n, nl, g, j):
                if j >= len(TAPS_DVE[g]):
                    return
                ky, kx = divmod(TAPS_DVE[g][j], 3)
                if j == 0:
                    dve.wait_ge(conv_s, n * 2 + (g + 1))
                else:
                    dve.wait_ge(tap_s, taps_before(n, g) + j)
                bank = conv_bank(g).rearrange("p (r c) -> p r c", c=W)
                nc.vector.scalar_tensor_tensor(
                    bank, xn[nl % 2][:, g, ky:ky + ROWS, kx:kx + W], dw_f[:, g, TAPS_DVE[g][j]:TAPS_DVE[g][j] + 1],
                    bank, ALU.mult, ALU.add).then_inc(tap_s, 1)

            dve.wait_ge(small_in, 32)
            nc.vector.tensor_copy(dw_hi[:], dw_f[:]).then_inc(taps_split, 1)
            dve.wait_ge(taps_split, 1)
            nc.vector.tensor_tensor(dw_lo[:], dw_f[:], dw_hi[:].bitcast(F32), ALU.subtract).then_inc(taps_split, 1)
            dve.wait_ge(taps_split, 2)
            dve.wait_ge(consts, 2)
            for g in range(HALVES):
                for j, t in enumerate(TAPS_PE[g]):
                    for diag, w in ((diag_hi, dw_hi[:].bitcast(F32)), (diag_lo, dw_lo[:])):
                        nc.vector.tensor_scalar(diag[:, g, j, :], ident[:], w[:, g, t:t + 1], None,
                                                ALU.mult).then_inc(taps_split, 1)
            dve.wait_ge(consts, CONSTS)
            group_stats(0)
            dve.wait_ge(weights_in, 16)
            nc.vector.tensor_copy(w_hi[:], w_raw).then_inc(split, 1)
            dve.wait_ge(split, 1)
            nc.vector.tensor_tensor(w_lo[:], w_raw, w_hi[:].bitcast(F32), ALU.subtract).then_inc(split, 1)
            dve.sem_inc(prod_s, PROD0)
            dve.sem_inc(acc_s, ACC0)
            for n in range(2):
                for g in range(HALVES):
                    for j in range(9):
                        tap(n, n, g, j)

            def body(n0, b0, last):
                for nl in range(STEPS):
                    t, par, n = nl % TILES, nl // TILES, n0 + nl
                    for g in range(HALVES):
                        q = (nl * 2 + g) * NP
                        taps = not (last and nl + 2 >= STEPS)

                        def beside(j):
                            if taps:
                                tap(n + 2, nl + 2, g, j)

                        multiply(n0, q, 0)
                        beside(0)
                        multiply(n0, q + 1, 1)
                        beside(1)
                        accumulate(n0, q + 1, 1)
                        beside(2)
                        multiply(n0, q + 2, 2)
                        beside(3)
                        accumulate(n0, q + 2, 2)
                        beside(4)
                        multiply(n0, q + 3, 3)
                        beside(5)
                        accumulate(n0, q + 3, 3)
                        for j in range(6, 9):
                            beside(j)
                        if (t, g) == (3, 0) and not (last and par):
                            group_stats(b0 + par + 1)

            loop(dve, body)

        @block.tensor
        def _(pe):
            def conv(n, nl, g):
                par, bank = nl % 2, conv_bank(g)
                pe.wait_ge(xhi_s, n + 1)
                if not (isinstance(n, int) and n == 0):
                    pe.wait_ge(gelu_s, n * 2 + (g - 1))

                def products(diag, xs, start, stop):
                    for j, t in enumerate(TAPS_PE[g]):
                        ky, kx = divmod(t, 3)
                        last = nc.tensor.matmul(bank, diag[:, g, j, :], xs[par][:, g, ky:ky + ROWS, kx:kx + W],
                                                start=start and j == 0, stop=stop and j == len(TAPS_PE[g]) - 1)
                    return last

                products(diag_hi, xhi, True, False)
                products(diag_lo, xhi, False, False)
                pe.wait_ge(xlo_s, n + 1)
                products(diag_hi, xlo, False, True).then_inc(conv_s, 1)

            def pointwise(n0, n, nl, q, k):
                par, g = nl % 2, (q // NP) % 2
                p = last_user(q)
                pl, pg, pk = p // (2 * NP), (p // NP) % 2, p % NP
                if 0 < pk <= ADDS[pg]:
                    pe.wait_ge(acc_s, added(n0, pl, pg) + pk)
                else:
                    pe.wait_ge(prod_s, n0 * (2 * NP) + (p + 1 + PROD0))
                if g == 0 and k == 0:
                    pe.wait_ge(hhi_s, n + 1)
                for side in range(2):
                    col = PAIRS[k][side] * C + g * P
                    steps = [(w, hhi, kk) for kk in range(HALVES) for w in (w_hi, w_lo)]
                    steps += [(w_hi, hlo, kk) for kk in range(HALVES)]
                    for s, (w, h, kk) in enumerate(steps):
                        if g == 0 and k == 0 and side == 0 and s == 2 * HALVES:
                            pe.wait_ge(hlo_s, n + 1)
                        last = nc.tensor.matmul(maps(q)[:, side, :], w[:, kk, col:col + P], h[par][:, kk, :],
                                                start=s == 0, stop=s == len(steps) - 1)
                    last.then_inc(maps_s, 1)

            pe.wait_ge(taps_split, 2 + 2 * sum(len(t) for t in TAPS_PE))
            for n in range(2):
                for g in range(HALVES):
                    conv(n, n, g)
            conv(2, 2, 0)
            pe.wait_ge(split, 2)

            def body(n0, b0, last):
                for nl in range(STEPS):
                    n = n0 + nl
                    for g in range(HALVES):
                        q = (nl * 2 + g) * NP
                        for k in range(NP):
                            pointwise(n0, n, nl, q + k, k)
                        ahead = 2 + g
                        if not (last and nl + ahead >= STEPS):
                            conv(n + ahead, nl + ahead, 1 - g)

            loop(pe, body)


def kernel(x, L0_conv_dw_weight, L0_conv_pw_weight, L0_conv_pw_bias):
    import numpy as np
    import concourse.bacc as bacc
    from concourse.bass_utils import run_bass_kernel_spmd

    x = np.ascontiguousarray(x)
    arrays = {
        "x": x,
        "pw_t": np.ascontiguousarray(np.asarray(L0_conv_pw_weight).T),
        "pw_b": np.ascontiguousarray(np.asarray(L0_conv_pw_bias).reshape(8, -1, 128).transpose(2, 1, 0)),
        "dw": np.ascontiguousarray(L0_conv_dw_weight).reshape(x.shape[1], 9),
    }
    nc = bacc.Bacc("TRN2", target_bir_lowering=False, num_devices=1)
    args = {k: nc.dram_tensor(k, a.shape, mybir.dt.from_np(a.dtype), kind="ExternalInput").ap()
            for k, a in arrays.items()}
    out = nc.dram_tensor("out", x.shape, mybir.dt.float32, kind="ExternalOutput").ap()
    preact_directional_conv(nc, out=out, **args)
    r = run_bass_kernel_spmd(nc, [arrays], core_ids=[0])
    return r.results[0]["out"]
```

```python
import concourse.bass as bass
from concourse import mybir
from contextlib import ExitStack


def preact_directional_conv(nc, x, pw_t, pw_b, dw, out):
    F32, F32R = mybir.dt.float32, mybir.dt.float32r
    ALU, ACT, AX = mybir.AluOpType, mybir.ActivationFunctionType, mybir.AxisListType

    P = 128
    B, C, H, W = x.shape
    HALVES = C // P
    DIRS = 8
    ROWS = 8
    TILES = H // ROWS
    PX = ROWS * W
    HP, WP = H + 2, W + 2
    TR = ROWS + 2
    PLANE = HP * WP
    GROUP = 8
    EPS = 1e-5
    STEPS = 2 * TILES
    BODIES = B // 2
    BANK = 512
    SLICES = 2
    SROWS = H // SLICES

    PAIRS = ((0, 1, WP), (2, 3, 1), (4, 7, WP + 1), (6, 5, WP - 1))
    NP = len(PAIRS)
    MAPS = DIRS + 1
    UNITS = HALVES * NP + 1
    LAST = UNITS - 1
    ADDS = HALVES * (NP - 1)
    TAPS = 9
    CENTER = TAPS // 2
    TAPS_DVE = tuple(t for t in range(TAPS) if t != CENTER)
    NT = len(TAPS_DVE)

    UNITS_BODY = STEPS * UNITS
    assert UNITS_BODY % 4 == 2
    GROUPS = [q % 4 for q in range(UNITS_BODY - 6)] + [0, 1, 2, 0, 1, 3]

    def last_user(q):
        p = q - 1
        while GROUPS[p % UNITS_BODY] != GROUPS[q]:
            p -= 1
        return p

    x_src = x.rearrange("b (g p) h w -> b g p h w", p=P)
    out_dst = out.rearrange("b (g p) h w -> b p g (h w)", p=P)

    ctx = ExitStack()
    with ctx:
        def sb(name, shape, dt=F32):
            return ctx.enter_context(nc.sbuf_tensor(name, shape, dt))

        def sem(name):
            return ctx.enter_context(nc.semaphore(name))

        def window(base, dims):
            return bass.AP(base.tensor, base.offset, [list(base.ap[0])] + [list(d) for d in dims])

        xpad_t = [sb(f"xpad{i}", [P, HALVES * PLANE]) for i in range(2)]
        xpad = [t[:].rearrange("p (g r c) -> p g r c", g=HALVES, c=WP) for t in xpad_t]
        xn = [sb(f"xn{i}", [P, HALVES, TR, WP]) for i in range(2)]
        dconv = [sb(f"dconv{i}", [P, HALVES, PX]) for i in range(2)]
        hid = [sb(f"hid{i}", [P, HALVES, PX]) for i in range(2)]
        hhi = [sb(f"hhi{i}", [P, HALVES, PX], F32R) for i in range(2)]
        hlo = [sb(f"hlo{i}", [P, HALVES, PX], F32R) for i in range(2)]
        acc = [sb(f"acc{i}", [P, HALVES, 2, PX]) for i in range(2)]
        products = sb("products", [P, ADDS + 1, 2, PX])
        outb = [sb(f"outb{i}", [P, HALVES, PX]) for i in range(2)]

        w_raw = xpad_t[1][:, 0:HALVES * MAPS * C].rearrange("p (k m) -> p k m", k=HALVES)
        w_hi = sb("w_hi", [P, HALVES, MAPS * C], F32R)
        w_lo = sb("w_lo", [P, HALVES, MAPS * C], F32R)
        dw_f = sb("dw_f", [P, HALVES, 9])
        pb_f = sb("pb_f", [P, HALVES, MAPS])
        zeros = sb("zeros", [P, HALVES, 1, WP])
        neg_half = sb("neg_half", [P, HALVES])
        ones = sb("ones", [P, HALVES])

        squares_out = sb("squares_out", [P, SROWS, W])
        part_sums = sb("part_sums", [P, HALVES, SLICES])
        part_neg = sb("part_neg", [P, HALVES, SLICES])
        part_sq = sb("part_sq", [P, HALVES, SLICES])
        neg_mean_c = sb("neg_mean_c", [P, HALVES])
        moments = sb("moments", [P, 32])
        mom_t = sb("mom_t", [P, 32])
        sums = sb("sums", [P, 4])
        mean_t = sb("mean_t", [P, 32])
        dev_t = sb("dev_t", [P, 32])
        devs_t = sb("devs_t", [P, 32])
        mean_b = sb("mean_b", [P, 32])
        devs_b = sb("devs_b", [P, 32])
        var_eps = sb("var_eps", [P, HALVES])
        neg_mean = sb("neg_mean", [P, HALVES])
        rstd = [sb(f"rstd{i}", [P, HALVES]) for i in range(2)]
        shift = [sb(f"shift{i}", [P, HALVES]) for i in range(2)]
        bias = [sb(f"bias{i}", [P, HALVES, MAPS]) for i in range(2)]

        psum = ctx.enter_context(nc.psum_tensor("psum", [P, 8, BANK], F32))

        def maps(q):
            b = 2 * GROUPS[q % UNITS_BODY]
            return psum[:, b:b + 2, 0:PX]

        def unit_map(u, side):
            if u == LAST:
                return DIRS, side
            return PAIRS[u % NP][side], u // NP

        weights_in = sem("weights_in")
        small_in = sem("small_in")
        x_in = [[sem(f"x_in{i}{g}") for g in range(HALVES)] for i in range(2)]
        out_sent = [sem(f"out_sent{i}") for i in range(2)]
        consts = sem("consts")
        split = sem("split")
        measure = sem("measure")
        stat = sem("stat")
        scales = sem("scales")
        wraps = sem("wraps")
        xn_s = sem("xn_s")
        start_s = sem("start_s")
        tap_s = sem("tap_s")
        gelu_s = sem("gelu_s")
        hhi_s = sem("hhi_s")
        hlo_s = sem("hlo_s")
        maps_s = sem("maps_s")
        biased_s = sem("biased_s")
        prod_s = sem("prod_s")
        added_s = sem("added_s")
        fold_s = sem("fold_s")
        final_s = sem("final_s")
        PROD0, ADD0, FOLD0, FINAL0, SENT0 = UNITS, ADDS, 2, 2, 16
        MEASURES = 2 * HALVES * SLICES + HALVES
        STAT = 14
        SCALES = 4
        CONSTS = 6
        SPLIT = 5

        GELU_AT, HHI_AT, NORM_AT, START_AT, WRAP_AT = 1, 2, (3, 4), (4, 5), 7
        SPLIT_H_AT, SCALES_AT = 3, 4
        STATS_AT = 4

        block = ctx.enter_context(nc.Block())

        def loop(engine, body):
            with engine.Fori(0, BODIES - 1) as i:
                body(i * STEPS, i * 2, False)
            body((BODIES - 1) * STEPS, (BODIES - 1) * 2, True)

        @block.sync
        def _(sp):
            def load_image(b, par):
                for g in range(HALVES):
                    sp.dma_start(xpad[par][:, g, 1:H + 1, 1:W + 1], x_src[b, g]).then_inc(x_in[par][g], 16)

            load_image(0, 0)
            for par in range(2):
                sp.sem_inc(out_sent[par], SENT0)
            sp.dma_start(dw_f[:], dw.rearrange("(g p) t -> p g t", p=P)).then_inc(small_in, 16)
            sp.dma_start(pb_f[:, :, 0:DIRS], pw_b).then_inc(small_in, 16)
            sp.dma_start(w_raw[:, :, 0:DIRS * C], pw_t.rearrange("(k p) m -> p k m", p=P)).then_inc(weights_in, 16)
            sp.wait_ge(split, SPLIT)

            def body(n0, b0, last):
                for nl in range(STEPS):
                    t, par = nl % TILES, (nl // TILES) % 2
                    if t == 0 and not (last and nl):
                        sp.wait_ge(final_s, n0 + (nl + FINAL0))
                        load_image(b0 + par + 1, 1 - par)
                    sp.wait_ge(final_s, n0 + (nl + 1 + FINAL0))
                    sp.dma_start(out_dst[b0 + par, :, :, t * PX:(t + 1) * PX],
                                 outb[nl % 2][:]).then_inc(out_sent[nl % 2], 16)

            loop(sp, body)
            for par in range(2):
                sp.wait_ge(out_sent[par], 16 * B * TILES // 2 + SENT0)

        @block.gpsimd
        def _(pool):
            nc.gpsimd.memset(neg_half[:], -0.5).then_inc(consts, 1)
            nc.gpsimd.memset(ones[:], 1.0).then_inc(consts, 1)
            nc.gpsimd.memset(zeros[:], 0.0).then_inc(consts, 1)
            nc.gpsimd.memset(moments[:], 0.0).then_inc(consts, 1)
            for par in range(2):
                nc.gpsimd.memset(xn[par][:], 0.0).then_inc(consts, 1)
            pool.sem_inc(final_s, FINAL0)
            pool.sem_inc(fold_s, FOLD0)
            pool.sem_inc(added_s, ADD0)

            def norm_scales(j, par):
                pool.wait_ge(stat, j * STAT + STAT)
                nc.gpsimd.tensor_tensor(rstd[par][:], var_eps[:], neg_half[:], ALU.pow).then_inc(scales, 1)
                pool.wait_ge(scales, j * SCALES + 1)
                nc.gpsimd.tensor_tensor(shift[par][:], neg_mean[:], rstd[par][:], ALU.mult).then_inc(scales, 1)
                nc.gpsimd.tensor_tensor(bias[par][:], pb_f[:], window(rstd[par][:], [[1, HALVES], [0, MAPS]]),
                                        ALU.mult).then_inc(scales, 1)
                pool.wait_ge(scales, j * SCALES + 3)
                nc.gpsimd.tensor_tensor(bias[par][:, :, DIRS], bias[par][:, :, DIRS], ones[:],
                                        ALU.add).then_inc(scales, 1)

            def split_h(n, nl):
                par = nl % 2
                pool.wait_ge(hhi_s, n + 1)
                nc.gpsimd.tensor_tensor(hlo[par][:], hid[par][:], hhi[par][:].bitcast(F32),
                                        ALU.subtract).then_inc(hlo_s, 1)

            def add_pair(n0, nl, g, k):
                pool.wait_ge(prod_s, n0 * UNITS + (nl * UNITS + g * NP + k + 1 + PROD0))
                i = g * (NP - 1) + k - 1
                if k > 1:
                    pool.wait_ge(added_s, n0 * ADDS + (nl * ADDS + i + ADD0))
                a = acc[nl % 2][:, g]
                nc.gpsimd.tensor_tensor(a, a, products[:, i], ALU.add).then_inc(added_s, 1)

            def finish(n0, nl):
                n, a, o = n0 + nl, acc[nl % 2], outb[nl % 2]
                pool.wait_ge(added_s, n0 * ADDS + ((nl + 1) * ADDS + ADD0))
                pool.wait_ge(out_sent[nl % 2], n0 * 8 + (16 * (nl // 2) + SENT0))
                nc.gpsimd.tensor_tensor(o[:], a[:, :, 0, :], a[:, :, 1, :], ALU.add).then_inc(fold_s, 1)
                pool.wait_ge(fold_s, n + (1 + FOLD0))
                pool.wait_ge(prod_s, n0 * UNITS + ((nl + 1) * UNITS + PROD0))
                nc.gpsimd.tensor_tensor(o[:], o[:], products[:, ADDS], ALU.add).then_inc(final_s, 1)

            pool.wait_ge(consts, CONSTS)
            pool.wait_ge(split, 1)
            norm_scales(0, 0)
            split_h(0, 0)

            def body(n0, b0, last):
                for nl in range(STEPS):
                    t, par = nl % TILES, nl // TILES
                    for i in range(ADDS):
                        if i == SPLIT_H_AT and not (last and nl + 1 >= STEPS):
                            split_h(n0 + (nl + 1), nl + 1)
                        add_pair(n0, nl, i // (NP - 1), i % (NP - 1) + 1)
                        if i == SCALES_AT and t == 3 and not (last and par):
                            norm_scales(b0 + par + 1, 1 - par)
                    finish(n0, nl)

            loop(pool, body)

        @block.scalar
        def _(act):
            def wrap(b, par):
                for g in range(HALVES):
                    act.wait_ge(x_in[par][g], (b - par) * 8 + 16)
                v = xpad[par]
                nc.scalar.copy(v[:, :, 1:H + 1, 0:1], v[:, :, 1:H + 1, W:W + 1]).then_inc(wraps, 1)
                nc.scalar.copy(v[:, :, 1:H + 1, W + 1:WP], v[:, :, 1:H + 1, 1:2]).then_inc(wraps, 1)
                act.wait_ge(wraps, b * 4 + 2)
                nc.scalar.copy(v[:, :, 0:1, :], v[:, :, H:H + 1, :]).then_inc(wraps, 1)
                nc.scalar.copy(v[:, :, H + 1:HP, :], v[:, :, 1:2, :]).then_inc(wraps, 1)

            def rows_of(par, g, c):
                return xpad[par][:, g, 1 + c * SROWS:1 + (c + 1) * SROWS, 1:W + 1]

            def measure_step(b, par, i):
                g, j = divmod(i, 2 * SLICES + 1)
                if j == 0:
                    act.wait_ge(x_in[par][g], (b - par) * 8 + 16)
                if i:
                    act.wait_ge(measure, b * MEASURES + i)
                elif not isinstance(b, int) or b:
                    act.wait_ge(stat, b * STAT)
                if j < SLICES:
                    nc.scalar.activation(squares_out[:], rows_of(par, g, j), ACT.Copy,
                                         accum_out=part_sums[:, g, j:j + 1]).then_inc(measure, 1)
                elif j == SLICES:
                    nc.scalar.activation(part_neg[:, g, :], part_sums[:, g, :], ACT.Copy, scale=-1.0 / (H * W),
                                         accum_out=neg_mean_c[:, g:g + 1]).then_inc(measure, 1)
                else:
                    j -= SLICES + 1
                    nc.scalar.activation(squares_out[:], rows_of(par, g, j), ACT.Square,
                                         bias=neg_mean_c[:, g:g + 1],
                                         accum_out=part_sq[:, g, j:j + 1]).then_inc(measure, 1)

            def normalise(nl, b, g):
                t, par, ip = nl % TILES, nl % 2, (nl // TILES) % 2
                r0, r1 = (1 if t == 0 else 0), (TR - 1 if t == TILES - 1 else TR)
                if g == 0 and t == 0:
                    nc.scalar.copy(xn[par][:, :, 0:1, :], zeros[:]).then_inc(xn_s, 1)
                    act.wait_ge(scales, b * SCALES + SCALES)
                if g == 0 and t == TILES - 1:
                    nc.scalar.copy(xn[par][:, :, TR - 1:TR, :], zeros[:]).then_inc(xn_s, 1)
                nc.scalar.activation(
                    xn[par][:, g, r0:r1, 1:W + 1], xpad[ip][:, g, t * ROWS + r0:t * ROWS + r1, 1:W + 1],
                    ACT.Identity, bias=shift[ip][:, g:g + 1], scale=rstd[ip][:, g:g + 1]).then_inc(xn_s, 1)

            def start_conv(n, nl, b, g):
                t, par = nl % TILES, nl % 2
                act.wait_ge(xn_s, b * (2 * TILES + 2) + (2 * t + g + 2 + (t == TILES - 1)))
                if nl >= 2 or not isinstance(n, int):
                    act.wait_ge(gelu_s, n - 1)
                nc.scalar.activation(dconv[par][:, g, :].rearrange("p (r c) -> p r c", c=W),
                                     xn[par][:, g, 1:1 + ROWS, 1:1 + W], ACT.Copy,
                                     scale=dw_f[:, g, CENTER:CENTER + 1]).then_inc(start_s, 1)

            def gelu(n, nl):
                act.wait_ge(tap_s, n * (2 * NT) + 2 * NT)
                nc.scalar.activation(hid[nl % 2][:], dconv[nl % 2][:], ACT.Gelu).then_inc(gelu_s, 1)

            def split_h_hi(n, nl):
                act.wait_ge(gelu_s, n + 1)
                nc.scalar.copy(hhi[nl % 2][:], hid[nl % 2][:]).then_inc(hhi_s, 1)

            def add_bias(n0, nl, u):
                ip, q = (nl // TILES) % 2, nl * UNITS + u
                for side in range(2):
                    d, g = unit_map(u, side)
                    act.wait_ge(maps_s, n0 * (2 * UNITS) + (2 * q + side + 1))
                    m = maps(q)[:, side, :]
                    nc.scalar.activation(m, m, ACT.Identity, bias=bias[ip][:, g, d:d + 1],
                                         scale=rstd[ip][:, g:g + 1]).then_inc(biased_s, 1)

            MEASURE_AT = ((1, 0), (1, 3), (1, 6), (1, 8), (2, 1), (2, 4), (2, 7), (3, 0), (3, 2), (3, 4))
            assert len(MEASURE_AT) == MEASURES
            for i in range(MEASURES):
                measure_step(0, 0, i)
            wrap(0, 0)
            act.wait_ge(consts, CONSTS)
            act.wait_ge(small_in, 32)
            for n in range(2):
                for g in range(HALVES):
                    normalise(n, 0, g)
                    start_conv(n, n, 0, g)
            gelu(0, 0)
            split_h_hi(0, 0)
            for g in range(HALVES):
                normalise(2, 0, g)
                start_conv(2, 2, 0, g)

            def body(n0, b0, last):
                for nl in range(STEPS):
                    t, par, n = nl % TILES, nl // TILES, n0 + nl
                    more = lambda k: not (last and nl + k >= STEPS)
                    b3 = b0 + (nl + 3) // TILES
                    for u in range(UNITS):
                        add_bias(n0, nl, u)
                        if (t, u) in MEASURE_AT and not (last and par):
                            measure_step(b0 + par + 1, 1 - par, MEASURE_AT.index((t, u)))
                        if u == GELU_AT and more(1):
                            gelu(n + 1, nl + 1)
                        if u == HHI_AT and more(1):
                            split_h_hi(n + 1, nl + 1)
                        for g in range(HALVES):
                            if u == NORM_AT[g] and more(3):
                                normalise(nl + 3, b3, g)
                            if u == START_AT[g] and more(3):
                                start_conv(n + 3, nl + 3, b3, g)
                        if u == WRAP_AT and t == 2 and not (last and par):
                            wrap(b0 + par + 1, 1 - par)

            loop(act, body)

        @block.vector
        def _(dve):
            def group_stats(b):
                done = [0]

                def then(ins):
                    ins.then_inc(stat, 1)
                    done[0] += 1

                def wait():
                    dve.wait_ge(stat, b * STAT + done[0])

                by8 = lambda v: v.rearrange("p (a e) -> p a e", e=GROUP)
                wide = lambda v: window(v, [[1, 32 // GROUP], [0, GROUP]])
                dve.wait_ge(measure, b * MEASURES + MEASURES)
                then(nc.vector.reduce_sum(sums[:, 0:HALVES], part_sq[:], axis=AX.X))
                then(nc.vector.tensor_scalar(moments[:, 0:3:2], neg_mean_c[:], -1.0, None, ALU.mult))
                wait()
                then(nc.vector.tensor_scalar(moments[:, 1:4:2], sums[:, 0:HALVES], 1.0 / (H * W), None, ALU.mult))
                wait()
                then(nc.vector.transpose(mom_t[:], moments[:]))
                wait()
                then(nc.vector.reduce_sum(sums[:], by8(mom_t[:]), axis=AX.X))
                wait()
                then(nc.vector.tensor_scalar(by8(mean_t[:]), wide(sums[:]), 1.0 / GROUP, None, ALU.mult))
                wait()
                then(nc.vector.tensor_tensor(dev_t[:], mom_t[:], mean_t[:], ALU.subtract))
                wait()
                then(nc.vector.tensor_tensor(dev_t[:], dev_t[:], dev_t[:], ALU.mult))
                wait()
                then(nc.vector.reduce_sum(sums[:], by8(dev_t[:]), axis=AX.X))
                wait()
                then(nc.vector.tensor_scalar(by8(devs_t[:]), wide(sums[:]), 1.0 / GROUP, None, ALU.mult))
                wait()
                then(nc.vector.transpose(mean_b[:], mean_t[:]))
                then(nc.vector.transpose(devs_b[:], devs_t[:]))
                wait()
                then(nc.vector.scalar_tensor_tensor(var_eps[:], mean_b[:, 1:4:2], EPS, devs_b[:, 0:3:2],
                                                    ALU.add, ALU.add))
                then(nc.vector.tensor_scalar(neg_mean[:], mean_b[:, 0:3:2], -1.0, None, ALU.mult))

            def multiply(n0, b, nl, u):
                t, ip, q = nl % TILES, (nl // TILES) % 2, nl * UNITS + u
                g, k = divmod(u, NP)
                if t == 0 and u == 0:
                    dve.wait_ge(wraps, b * 4 + 4)
                if u == 0:
                    dve.wait_ge(fold_s, n0 + (nl - 1 + FOLD0))
                if u == LAST:
                    dve.wait_ge(final_s, n0 + (nl + FINAL0))
                    to = products[:, ADDS]
                elif k == 0:
                    to = acc[nl % 2][:, g]
                else:
                    i = g * (NP - 1) + k - 1
                    dve.wait_ge(added_s, n0 * ADDS + (nl * ADDS + (i + 1 - ADDS) + ADD0))
                    to = products[:, i]
                at = (t * ROWS + 1) * WP + 1
                if u == LAST:
                    step = PLANE
                else:
                    at += g * PLANE - PAIRS[k][2]
                    step = 2 * PAIRS[k][2]
                dve.wait_ge(biased_s, n0 * (2 * UNITS) + (2 * q + 2))
                nc.vector.tensor_tensor(to.rearrange("p s (r c) -> p s r c", c=W),
                                        maps(q).rearrange("p s (r c) -> p s r c", c=W),
                                        window(xpad_t[ip][:, at:at + 1], [[step, 2], [WP, ROWS], [1, W]]),
                                        ALU.mult).then_inc(prod_s, 1)

            def tap(n, nl, g, j):
                ky, kx = divmod(TAPS_DVE[j], 3)
                if j == 0:
                    dve.wait_ge(start_s, n * 2 + (g + 1))
                else:
                    dve.wait_ge(tap_s, n * (2 * NT) + (2 * (j - 1) + g + 1))
                d = dconv[nl % 2][:, g, :].rearrange("p (r c) -> p r c", c=W)
                nc.vector.scalar_tensor_tensor(
                    d, xn[nl % 2][:, g, ky:ky + ROWS, kx:kx + W], dw_f[:, g, TAPS_DVE[j]:TAPS_DVE[j] + 1],
                    d, ALU.mult, ALU.add).then_inc(tap_s, 1)

            dve.wait_ge(small_in, 32)
            nc.vector.reduce_sum(pb_f[:, :, DIRS], pb_f[:, :, 0:DIRS], axis=AX.X, negate=True).then_inc(split, 1)
            dve.wait_ge(weights_in, 16)
            for k in range(HALVES):
                nc.vector.reduce_sum(w_raw[:, k, DIRS * C:], window(w_raw[:, k, 0:1], [[1, C], [C, DIRS]]),
                                     axis=AX.X, negate=True).then_inc(split, 1)
            dve.wait_ge(split, 1 + HALVES)
            nc.vector.tensor_copy(w_hi[:], w_raw).then_inc(split, 1)
            dve.wait_ge(split, 2 + HALVES)
            nc.vector.tensor_tensor(w_lo[:], w_raw, w_hi[:].bitcast(F32), ALU.subtract).then_inc(split, 1)
            dve.wait_ge(consts, CONSTS)
            group_stats(0)
            dve.sem_inc(prod_s, PROD0)
            for n in range(2):
                for j in range(NT):
                    for g in range(HALVES):
                        tap(n, n, g, j)

            def body(n0, b0, last):
                for nl in range(STEPS):
                    t, par, n = nl % TILES, nl // TILES, n0 + nl
                    for u in range(UNITS):
                        multiply(n0, b0 + par, nl, u)
                        if u < NT and not (last and nl + 2 >= STEPS):
                            for g in range(HALVES):
                                tap(n + 2, nl + 2, g, u)
                        if (t, u) == (3, STATS_AT) and not (last and par):
                            group_stats(b0 + par + 1)

            loop(dve, body)

        @block.tensor
        def _(pe):
            def make_maps(n0, nl, u):
                n, par, q = n0 + nl, nl % 2, nl * UNITS + u
                pe.wait_ge(prod_s, n0 * UNITS + (last_user(q) + 1 + PROD0))
                if u == 0:
                    pe.wait_ge(hhi_s, n + 1)
                for side in range(2):
                    d, g = unit_map(u, side)
                    col = d * C + g * P
                    steps = [(w, hhi, kk) for kk in range(HALVES) for w in (w_hi, w_lo)]
                    steps += [(w_hi, hlo, kk) for kk in range(HALVES)]
                    for s, (w, h, kk) in enumerate(steps):
                        if u == 0 and side == 0 and s == 2 * HALVES:
                            pe.wait_ge(hlo_s, n + 1)
                        last = nc.tensor.matmul(maps(q)[:, side, :], w[:, kk, col:col + P], h[par][:, kk, :],
                                                start=s == 0, stop=s == len(steps) - 1)
                    last.then_inc(maps_s, 1)

            pe.wait_ge(split, SPLIT)

            def body(n0, b0, last):
                for nl in range(STEPS):
                    for u in range(UNITS):
                        make_maps(n0, nl, u)

            loop(pe, body)


def kernel(x, L0_conv_dw_weight, L0_conv_pw_weight, L0_conv_pw_bias):
    import numpy as np
    import concourse.bacc as bacc
    from concourse.bass_utils import run_bass_kernel_spmd

    x = np.ascontiguousarray(x)
    arrays = {
        "x": x,
        "pw_t": np.ascontiguousarray(np.asarray(L0_conv_pw_weight).T),
        "pw_b": np.ascontiguousarray(np.asarray(L0_conv_pw_bias).reshape(8, -1, 128).transpose(2, 1, 0)),
        "dw": np.ascontiguousarray(L0_conv_dw_weight).reshape(x.shape[1], 9),
    }
    nc = bacc.Bacc("TRN2", target_bir_lowering=False, num_devices=1)
    args = {k: nc.dram_tensor(k, a.shape, mybir.dt.from_np(a.dtype), kind="ExternalInput").ap()
            for k, a in arrays.items()}
    out = nc.dram_tensor("out", x.shape, mybir.dt.float32, kind="ExternalOutput").ap()
    preact_directional_conv(nc, out=out, **args)
    r = run_bass_kernel_spmd(nc, [arrays], core_ids=[0])
    return r.results[0]["out"]
```

```python
import concourse.bass as bass
from concourse import mybir
from contextlib import ExitStack


def preact_directional_conv(nc, x, pw_t, pw_b, dw, out):
    F32, F32R = mybir.dt.float32, mybir.dt.float32r
    ALU, ACT, AX = mybir.AluOpType, mybir.ActivationFunctionType, mybir.AxisListType

    P = 128
    B, C, H, W = x.shape
    HALVES = C // P
    DIRS = 8
    ROWS = 8
    TILES = H // ROWS
    PX = ROWS * W
    HP, WP = H + 2, W + 2
    TR = ROWS + 2
    PLANE = HP * WP
    GROUP = 8
    EPS = 1e-5
    STEPS = 2 * TILES
    BODIES = B // 2
    BANK = 512
    SLICES = 2
    SROWS = H // SLICES

    PAIRS = ((0, 1, WP), (2, 3, 1), (4, 7, WP + 1), (6, 5, WP - 1))
    NP = len(PAIRS)
    MAPS = DIRS + 1
    UNITS = HALVES * NP + 1
    LAST = UNITS - 1
    ADDS = HALVES * (NP - 1)
    TAPS = 9
    CENTER = TAPS // 2
    TAPS_DVE = tuple(t for t in range(TAPS) if t != CENTER)
    NT = len(TAPS_DVE)

    UNITS_BODY = STEPS * UNITS
    assert UNITS_BODY % 4 == 2
    GROUPS = [q % 4 for q in range(UNITS_BODY - 6)] + [0, 1, 2, 0, 1, 3]

    def last_user(q):
        p = q - 1
        while GROUPS[p % UNITS_BODY] != GROUPS[q]:
            p -= 1
        return p

    x_src = x.rearrange("b (g p) h w -> b g p h w", p=P)
    out_dst = out.rearrange("b (g p) h w -> b p g (h w)", p=P)

    ctx = ExitStack()
    with ctx:
        def sb(name, shape, dt=F32):
            return ctx.enter_context(nc.sbuf_tensor(name, shape, dt))

        def sem(name):
            return ctx.enter_context(nc.semaphore(name))

        def window(base, dims):
            return bass.AP(base.tensor, base.offset, [list(base.ap[0])] + [list(d) for d in dims])

        xpad_t = [sb(f"xpad{i}", [P, HALVES * PLANE]) for i in range(2)]
        xpad = [t[:].rearrange("p (g r c) -> p g r c", g=HALVES, c=WP) for t in xpad_t]
        xn = [sb(f"xn{i}", [P, HALVES, TR, WP]) for i in range(2)]
        dconv = [sb(f"dconv{i}", [P, HALVES, PX]) for i in range(2)]
        hid = [sb(f"hid{i}", [P, HALVES, PX]) for i in range(2)]
        hhi = [sb(f"hhi{i}", [P, HALVES, PX], F32R) for i in range(2)]
        hlo = [sb(f"hlo{i}", [P, HALVES, PX], F32R) for i in range(2)]
        acc = [sb(f"acc{i}", [P, HALVES, 2, PX]) for i in range(2)]
        products = sb("products", [P, ADDS + 1, 2, PX])
        assert (ADDS + 1) * 2 * PX >= HALVES * H * W
        first = products[:].rearrange("p a s x -> p (a s x)")[:, 0:HALVES * H * W]
        first = first.rearrange("p (g c r w) -> p g c r w", g=HALVES, c=SLICES, w=W)
        outb = [sb(f"outb{i}", [P, HALVES, PX]) for i in range(2)]

        w_raw = xpad_t[1][:, 0:HALVES * MAPS * C].rearrange("p (k m) -> p k m", k=HALVES)
        w_dirs, w_ninth = slice(0, DIRS * C), slice(DIRS * C, MAPS * C)
        w_hi = sb("w_hi", [P, HALVES, MAPS * C], F32R)
        w_lo = sb("w_lo", [P, HALVES, MAPS * C], F32R)
        dw_f = sb("dw_f", [P, HALVES, 9])
        pb_f = sb("pb_f", [P, HALVES, MAPS])
        zeros = sb("zeros", [P, HALVES, 1, WP])
        neg_half = sb("neg_half", [P, HALVES])
        ones = sb("ones", [P, HALVES])

        squares_out = sb("squares_out", [P, SROWS, W])
        part_sums = sb("part_sums", [P, HALVES, SLICES])
        part_neg = sb("part_neg", [P, HALVES, SLICES])
        part_sq = sb("part_sq", [P, HALVES, SLICES])
        neg_mean_c = sb("neg_mean_c", [P, HALVES])
        moments = sb("moments", [P, 32])
        mom_t = sb("mom_t", [P, 32])
        sums = sb("sums", [P, 4])
        mean_t = sb("mean_t", [P, 32])
        dev_t = sb("dev_t", [P, 32])
        devs_t = sb("devs_t", [P, 32])
        mean_b = sb("mean_b", [P, 32])
        devs_b = sb("devs_b", [P, 32])
        var_eps = sb("var_eps", [P, HALVES])
        neg_mean = sb("neg_mean", [P, HALVES])
        rstd = [sb(f"rstd{i}", [P, HALVES]) for i in range(2)]
        shift = [sb(f"shift{i}", [P, HALVES]) for i in range(2)]
        bias = [sb(f"bias{i}", [P, HALVES, MAPS]) for i in range(2)]

        psum = ctx.enter_context(nc.psum_tensor("psum", [P, 8, BANK], F32))

        def rows_of(par, g, c):
            return xpad[par][:, g, 1 + c * SROWS:1 + (c + 1) * SROWS, 1:W + 1]

        def maps(q):
            b = 2 * GROUPS[q % UNITS_BODY]
            return psum[:, b:b + 2, 0:PX]

        def unit_map(u, side):
            if u == LAST:
                return DIRS, side
            return PAIRS[u % NP][side], u // NP

        weights_in = sem("weights_in")
        small_in = sem("small_in")
        first_in = [[sem(f"first_in{g}{c}") for c in range(SLICES)] for g in range(HALVES)]
        x_in = [[sem(f"x_in{i}{g}") for g in range(HALVES)] for i in range(2)]
        out_sent = [sem(f"out_sent{i}") for i in range(2)]
        consts = sem("consts")
        pb_sum = sem("pb_sum")
        w_hi_s = sem("w_hi_s")
        w_lo_s = sem("w_lo_s")
        ninth_s = sem("ninth_s")
        first_s = sem("first_s")
        measure = sem("measure")
        stat = sem("stat")
        scales = sem("scales")
        wraps = sem("wraps")
        xn_s = sem("xn_s")
        start_s = sem("start_s")
        tap_s = sem("tap_s")
        gelu_s = sem("gelu_s")
        hhi_s = sem("hhi_s")
        hlo_s = sem("hlo_s")
        maps_s = sem("maps_s")
        biased_s = sem("biased_s")
        prod_s = sem("prod_s")
        added_s = sem("added_s")
        fold_s = sem("fold_s")
        final_s = sem("final_s")
        PROD0, ADD0, FOLD0, FINAL0, SENT0 = UNITS, ADDS, 2, 2, 16
        MEASURES = 2 * HALVES * SLICES + HALVES
        STAT = 14
        SCALES = 4
        CONSTS = 6
        NINTH = DIRS + 2
        HALF_STEPS = 2 * SLICES + 1

        GELU_AT, HHI_AT, NORM_AT, START_AT, WRAP_AT = 1, 2, (3, 4), (4, 5), 7
        SPLIT_H_AT, SCALES_AT = 3, 4
        STATS_AT = 4

        block = ctx.enter_context(nc.Block())

        def loop(engine, body):
            with engine.Fori(0, BODIES - 1) as i:
                body(i * STEPS, i * 2, False)
            body((BODIES - 1) * STEPS, (BODIES - 1) * 2, True)

        @block.sync
        def _(sp):
            def load_image(b, par):
                for g in range(HALVES):
                    sp.dma_start(xpad[par][:, g, 1:H + 1, 1:W + 1], x_src[b, g]).then_inc(x_in[par][g], 16)

            for g in range(HALVES):
                for c in range(SLICES):
                    sp.dma_start(first[:, g, c], x_src[0, g, :, c * SROWS:(c + 1) * SROWS, :]).then_inc(
                        first_in[g][c], 16)
            for par in range(2):
                sp.sem_inc(out_sent[par], SENT0)
            sp.dma_start(dw_f[:], dw.rearrange("(g p) t -> p g t", p=P)).then_inc(small_in, 16)
            sp.dma_start(pb_f[:, :, 0:DIRS], pw_b).then_inc(small_in, 16)
            sp.dma_start(w_raw[:, :, 0:DIRS * C], pw_t.rearrange("(k p) m -> p k m", p=P)).then_inc(weights_in, 16)
            sp.wait_ge(w_lo_s, 1)
            sp.wait_ge(ninth_s, NINTH)

            def body(n0, b0, last):
                for nl in range(STEPS):
                    t, par = nl % TILES, (nl // TILES) % 2
                    if t == 0 and not (last and nl):
                        sp.wait_ge(final_s, n0 + (nl + FINAL0))
                        load_image(b0 + par + 1, 1 - par)
                    sp.wait_ge(final_s, n0 + (nl + 1 + FINAL0))
                    sp.dma_start(out_dst[b0 + par, :, :, t * PX:(t + 1) * PX],
                                 outb[nl % 2][:]).then_inc(out_sent[nl % 2], 16)

            loop(sp, body)
            for par in range(2):
                sp.wait_ge(out_sent[par], 16 * B * TILES // 2 + SENT0)

        @block.gpsimd
        def _(pool):
            nc.gpsimd.memset(neg_half[:], -0.5).then_inc(consts, 1)
            nc.gpsimd.memset(ones[:], 1.0).then_inc(consts, 1)
            nc.gpsimd.memset(zeros[:], 0.0).then_inc(consts, 1)
            nc.gpsimd.memset(moments[:], 0.0).then_inc(consts, 1)
            for par in range(2):
                nc.gpsimd.memset(xn[par][:], 0.0).then_inc(consts, 1)
            pool.sem_inc(final_s, FINAL0)
            pool.sem_inc(fold_s, FOLD0)
            pool.sem_inc(added_s, ADD0)
            for c in range(SLICES):
                pool.wait_ge(first_in[0][c], 16)
                nc.gpsimd.tensor_copy(rows_of(0, 0, c), first[:, 0, c]).then_inc(x_in[0][0], 16 // SLICES)

            def norm_scales(j, par):
                pool.wait_ge(stat, j * STAT + STAT)
                nc.gpsimd.tensor_tensor(rstd[par][:], var_eps[:], neg_half[:], ALU.pow).then_inc(scales, 1)
                pool.wait_ge(scales, j * SCALES + 1)
                nc.gpsimd.tensor_tensor(shift[par][:], neg_mean[:], rstd[par][:], ALU.mult).then_inc(scales, 1)
                nc.gpsimd.tensor_tensor(bias[par][:], pb_f[:], window(rstd[par][:], [[1, HALVES], [0, MAPS]]),
                                        ALU.mult).then_inc(scales, 1)
                pool.wait_ge(scales, j * SCALES + 3)
                nc.gpsimd.tensor_tensor(bias[par][:, :, DIRS], bias[par][:, :, DIRS], ones[:],
                                        ALU.add).then_inc(scales, 1)

            def split_h(n, nl):
                par = nl % 2
                pool.wait_ge(hhi_s, n + 1)
                nc.gpsimd.tensor_tensor(hlo[par][:], hid[par][:], hhi[par][:].bitcast(F32),
                                        ALU.subtract).then_inc(hlo_s, 1)

            def add_pair(n0, nl, g, k):
                pool.wait_ge(prod_s, n0 * UNITS + (nl * UNITS + g * NP + k + 1 + PROD0))
                i = g * (NP - 1) + k - 1
                if k > 1:
                    pool.wait_ge(added_s, n0 * ADDS + (nl * ADDS + i + ADD0))
                a = acc[nl % 2][:, g]
                nc.gpsimd.tensor_tensor(a, a, products[:, i], ALU.add).then_inc(added_s, 1)

            def finish(n0, nl):
                n, a, o = n0 + nl, acc[nl % 2], outb[nl % 2]
                pool.wait_ge(added_s, n0 * ADDS + ((nl + 1) * ADDS + ADD0))
                pool.wait_ge(out_sent[nl % 2], n0 * 8 + (16 * (nl // 2) + SENT0))
                nc.gpsimd.tensor_tensor(o[:], a[:, :, 0, :], a[:, :, 1, :], ALU.add).then_inc(fold_s, 1)
                pool.wait_ge(fold_s, n + (1 + FOLD0))
                pool.wait_ge(prod_s, n0 * UNITS + ((nl + 1) * UNITS + PROD0))
                nc.gpsimd.tensor_tensor(o[:], o[:], products[:, ADDS], ALU.add).then_inc(final_s, 1)

            pool.wait_ge(consts, CONSTS)
            pool.wait_ge(pb_sum, 1)
            norm_scales(0, 0)
            pool.wait_ge(w_hi_s, 1)
            nc.gpsimd.tensor_tensor(w_lo[:, :, w_dirs], w_raw[:, :, w_dirs], w_hi[:, :, w_dirs].bitcast(F32),
                                    ALU.subtract).then_inc(w_lo_s, 1)
            w9 = w_raw[:, :, w_ninth]
            for d in range(1, DIRS):
                if d == DIRS // 2:
                    split_h(0, 0)
                pool.wait_ge(ninth_s, d)
                nc.gpsimd.tensor_tensor(w9, w9, w_raw[:, :, d * C:(d + 1) * C], ALU.subtract).then_inc(ninth_s, 1)
            pool.wait_ge(ninth_s, DIRS)
            nc.gpsimd.tensor_copy(w_hi[:, :, w_ninth], w9).then_inc(ninth_s, 1)
            pool.wait_ge(ninth_s, DIRS + 1)
            nc.gpsimd.tensor_tensor(w_lo[:, :, w_ninth], w9, w_hi[:, :, w_ninth].bitcast(F32),
                                    ALU.subtract).then_inc(ninth_s, 1)

            def body(n0, b0, last):
                for nl in range(STEPS):
                    t, par = nl % TILES, nl // TILES
                    for i in range(ADDS):
                        if i == SPLIT_H_AT and not (last and nl + 1 >= STEPS):
                            split_h(n0 + (nl + 1), nl + 1)
                        add_pair(n0, nl, i // (NP - 1), i % (NP - 1) + 1)
                        if i == SCALES_AT and t == 3 and not (last and par):
                            norm_scales(b0 + par + 1, 1 - par)
                    finish(n0, nl)

            loop(pool, body)

        @block.scalar
        def _(act):
            def wrap(b, par):
                for g in range(HALVES):
                    act.wait_ge(x_in[par][g], (b - par) * 8 + 16)
                v = xpad[par]
                nc.scalar.copy(v[:, :, 1:H + 1, 0:1], v[:, :, 1:H + 1, W:W + 1]).then_inc(wraps, 1)
                nc.scalar.copy(v[:, :, 1:H + 1, W + 1:WP], v[:, :, 1:H + 1, 1:2]).then_inc(wraps, 1)
                act.wait_ge(wraps, b * 4 + 2)
                nc.scalar.copy(v[:, :, 0:1, :], v[:, :, H:H + 1, :]).then_inc(wraps, 1)
                nc.scalar.copy(v[:, :, H + 1:HP, :], v[:, :, 1:2, :]).then_inc(wraps, 1)

            def slice_sum(rows, g, c):
                nc.scalar.activation(squares_out[:], rows, ACT.Copy,
                                     accum_out=part_sums[:, g, c:c + 1]).then_inc(measure, 1)

            def minus_mean(g):
                nc.scalar.activation(part_neg[:, g, :], part_sums[:, g, :], ACT.Copy, scale=-1.0 / (H * W),
                                     accum_out=neg_mean_c[:, g:g + 1]).then_inc(measure, 1)

            def slice_squares(rows, g, c):
                nc.scalar.activation(squares_out[:], rows, ACT.Square, bias=neg_mean_c[:, g:g + 1],
                                     accum_out=part_sq[:, g, c:c + 1]).then_inc(measure, 1)

            def measure_step(b, par, i):
                g, j = divmod(i, HALF_STEPS)
                if j == 0:
                    act.wait_ge(x_in[par][g], (b - par) * 8 + 16)
                if i:
                    act.wait_ge(measure, b * MEASURES + i)
                else:
                    act.wait_ge(stat, b * STAT)
                if j < SLICES:
                    slice_sum(rows_of(par, g, j), g, j)
                elif j == SLICES:
                    minus_mean(g)
                else:
                    slice_squares(rows_of(par, g, j - SLICES - 1), g, j - SLICES - 1)

            def measure_first():
                for i in range(HALF_STEPS):
                    if i < SLICES:
                        act.wait_ge(first_in[0][i], 16)
                    if i:
                        act.wait_ge(measure, i)
                    if i < SLICES:
                        slice_sum(first[:, 0, i], 0, i)
                    elif i == SLICES:
                        minus_mean(0)
                    else:
                        slice_squares(first[:, 0, i - SLICES - 1], 0, i - SLICES - 1)
                for c in range(SLICES):
                    act.wait_ge(first_in[1][c], 16)
                    nc.scalar.copy(rows_of(0, 1, c), first[:, 1, c]).then_inc(x_in[0][1], 16 // SLICES)
                act.wait_ge(first_s, SLICES + 2)
                act.wait_ge(measure, HALF_STEPS)
                slice_squares(first[:, 1, SLICES - 1], 1, SLICES - 1)
                act.sem_inc(measure, MEASURES - HALF_STEPS - 1)

            def normalise(nl, b, g):
                t, par, ip = nl % TILES, nl % 2, (nl // TILES) % 2
                r0, r1 = (1 if t == 0 else 0), (TR - 1 if t == TILES - 1 else TR)
                if g == 0 and t == 0:
                    nc.scalar.copy(xn[par][:, :, 0:1, :], zeros[:]).then_inc(xn_s, 1)
                    act.wait_ge(scales, b * SCALES + SCALES)
                if g == 0 and t == TILES - 1:
                    nc.scalar.copy(xn[par][:, :, TR - 1:TR, :], zeros[:]).then_inc(xn_s, 1)
                nc.scalar.activation(
                    xn[par][:, g, r0:r1, 1:W + 1], xpad[ip][:, g, t * ROWS + r0:t * ROWS + r1, 1:W + 1],
                    ACT.Identity, bias=shift[ip][:, g:g + 1], scale=rstd[ip][:, g:g + 1]).then_inc(xn_s, 1)

            def start_conv(n, nl, b, g):
                t, par = nl % TILES, nl % 2
                act.wait_ge(xn_s, b * (2 * TILES + 2) + (2 * t + g + 2 + (t == TILES - 1)))
                if nl >= 2 or not isinstance(n, int):
                    act.wait_ge(gelu_s, n - 1)
                nc.scalar.activation(dconv[par][:, g, :].rearrange("p (r c) -> p r c", c=W),
                                     xn[par][:, g, 1:1 + ROWS, 1:1 + W], ACT.Copy,
                                     scale=dw_f[:, g, CENTER:CENTER + 1]).then_inc(start_s, 1)

            def gelu(n, nl):
                act.wait_ge(tap_s, n * (2 * NT) + 2 * NT)
                nc.scalar.activation(hid[nl % 2][:], dconv[nl % 2][:], ACT.Gelu).then_inc(gelu_s, 1)

            def split_h_hi(n, nl):
                act.wait_ge(gelu_s, n + 1)
                nc.scalar.copy(hhi[nl % 2][:], hid[nl % 2][:]).then_inc(hhi_s, 1)

            def add_bias(n0, nl, u):
                ip, q = (nl // TILES) % 2, nl * UNITS + u
                for side in range(2):
                    d, g = unit_map(u, side)
                    act.wait_ge(maps_s, n0 * (2 * UNITS) + (2 * q + side + 1))
                    m = maps(q)[:, side, :]
                    nc.scalar.activation(m, m, ACT.Identity, bias=bias[ip][:, g, d:d + 1],
                                         scale=rstd[ip][:, g:g + 1]).then_inc(biased_s, 1)

            MEASURE_AT = ((1, 0), (1, 3), (1, 6), (1, 8), (2, 1), (2, 4), (2, 7), (3, 0), (3, 2), (3, 4))
            assert len(MEASURE_AT) == MEASURES
            measure_first()
            wrap(0, 0)
            act.wait_ge(weights_in, 16)
            nc.scalar.activation(w_raw[:, :, w_ninth], w_raw[:, :, 0:C], ACT.Copy, scale=-1.0).then_inc(ninth_s, 1)
            act.wait_ge(consts, CONSTS)
            act.wait_ge(small_in, 32)
            for n in range(2):
                for g in range(HALVES):
                    normalise(n, 0, g)
                    start_conv(n, n, 0, g)
            gelu(0, 0)
            split_h_hi(0, 0)
            for g in range(HALVES):
                normalise(2, 0, g)
                start_conv(2, 2, 0, g)

            def body(n0, b0, last):
                for nl in range(STEPS):
                    t, par, n = nl % TILES, nl // TILES, n0 + nl
                    more = lambda k: not (last and nl + k >= STEPS)
                    b3 = b0 + (nl + 3) // TILES
                    for u in range(UNITS):
                        add_bias(n0, nl, u)
                        if (t, u) in MEASURE_AT and not (last and par):
                            measure_step(b0 + par + 1, 1 - par, MEASURE_AT.index((t, u)))
                        if u == GELU_AT and more(1):
                            gelu(n + 1, nl + 1)
                        if u == HHI_AT and more(1):
                            split_h_hi(n + 1, nl + 1)
                        for g in range(HALVES):
                            if u == NORM_AT[g] and more(3):
                                normalise(nl + 3, b3, g)
                            if u == START_AT[g] and more(3):
                                start_conv(n + 3, nl + 3, b3, g)
                        if u == WRAP_AT and t == 2 and not (last and par):
                            wrap(b0 + par + 1, 1 - par)

            loop(act, body)

        @block.vector
        def _(dve):
            def group_stats(b):
                done = [0]

                def then(ins):
                    ins.then_inc(stat, 1)
                    done[0] += 1

                def wait():
                    dve.wait_ge(stat, b * STAT + done[0])

                by8 = lambda v: v.rearrange("p (a e) -> p a e", e=GROUP)
                wide = lambda v: window(v, [[1, 32 // GROUP], [0, GROUP]])
                dve.wait_ge(measure, b * MEASURES + MEASURES)
                then(nc.vector.reduce_sum(sums[:, 0:HALVES], part_sq[:], axis=AX.X))
                then(nc.vector.tensor_scalar(moments[:, 0:3:2], neg_mean_c[:], -1.0, None, ALU.mult))
                wait()
                then(nc.vector.tensor_scalar(moments[:, 1:4:2], sums[:, 0:HALVES], 1.0 / (H * W), None, ALU.mult))
                wait()
                then(nc.vector.transpose(mom_t[:], moments[:]))
                wait()
                then(nc.vector.reduce_sum(sums[:], by8(mom_t[:]), axis=AX.X))
                wait()
                then(nc.vector.tensor_scalar(by8(mean_t[:]), wide(sums[:]), 1.0 / GROUP, None, ALU.mult))
                wait()
                then(nc.vector.tensor_tensor(dev_t[:], mom_t[:], mean_t[:], ALU.subtract))
                wait()
                then(nc.vector.tensor_tensor(dev_t[:], dev_t[:], dev_t[:], ALU.mult))
                wait()
                then(nc.vector.reduce_sum(sums[:], by8(dev_t[:]), axis=AX.X))
                wait()
                then(nc.vector.tensor_scalar(by8(devs_t[:]), wide(sums[:]), 1.0 / GROUP, None, ALU.mult))
                wait()
                then(nc.vector.transpose(mean_b[:], mean_t[:]))
                then(nc.vector.transpose(devs_b[:], devs_t[:]))
                wait()
                then(nc.vector.scalar_tensor_tensor(var_eps[:], mean_b[:, 1:4:2], EPS, devs_b[:, 0:3:2],
                                                    ALU.add, ALU.add))
                then(nc.vector.tensor_scalar(neg_mean[:], mean_b[:, 0:3:2], -1.0, None, ALU.mult))

            def multiply(n0, b, nl, u):
                t, ip, q = nl % TILES, (nl // TILES) % 2, nl * UNITS + u
                g, k = divmod(u, NP)
                if t == 0 and u == 0:
                    dve.wait_ge(wraps, b * 4 + 4)
                if u == 0:
                    dve.wait_ge(fold_s, n0 + (nl - 1 + FOLD0))
                if u == LAST:
                    dve.wait_ge(final_s, n0 + (nl + FINAL0))
                    to = products[:, ADDS]
                elif k == 0:
                    to = acc[nl % 2][:, g]
                else:
                    i = g * (NP - 1) + k - 1
                    dve.wait_ge(added_s, n0 * ADDS + (nl * ADDS + (i + 1 - ADDS) + ADD0))
                    to = products[:, i]
                at = (t * ROWS + 1) * WP + 1
                if u == LAST:
                    step = PLANE
                else:
                    at += g * PLANE - PAIRS[k][2]
                    step = 2 * PAIRS[k][2]
                dve.wait_ge(biased_s, n0 * (2 * UNITS) + (2 * q + 2))
                nc.vector.tensor_tensor(to.rearrange("p s (r c) -> p s r c", c=W),
                                        maps(q).rearrange("p s (r c) -> p s r c", c=W),
                                        window(xpad_t[ip][:, at:at + 1], [[step, 2], [WP, ROWS], [1, W]]),
                                        ALU.mult).then_inc(prod_s, 1)

            def tap(n, nl, g, j):
                ky, kx = divmod(TAPS_DVE[j], 3)
                if j == 0:
                    dve.wait_ge(start_s, n * 2 + (g + 1))
                else:
                    dve.wait_ge(tap_s, n * (2 * NT) + (2 * (j - 1) + g + 1))
                d = dconv[nl % 2][:, g, :].rearrange("p (r c) -> p r c", c=W)
                nc.vector.scalar_tensor_tensor(
                    d, xn[nl % 2][:, g, ky:ky + ROWS, kx:kx + W], dw_f[:, g, TAPS_DVE[j]:TAPS_DVE[j] + 1],
                    d, ALU.mult, ALU.add).then_inc(tap_s, 1)

            def measure_first():
                centered = acc[0][:].rearrange("p g s x -> p (g s x)")[:, 0:SROWS * W]
                for c in range(SLICES):
                    dve.wait_ge(first_in[1][c], 16)
                    nc.vector.reduce_sum(part_sums[:, 1, c:c + 1], first[:, 1, c].rearrange("p r w -> p (r w)"),
                                         axis=AX.X).then_inc(first_s, 1)
                dve.wait_ge(first_s, SLICES)
                nc.vector.reduce_sum(sums[:, 0:1], part_sums[:, 1, :], axis=AX.X).then_inc(first_s, 1)
                dve.wait_ge(first_s, SLICES + 1)
                nc.vector.tensor_scalar(neg_mean_c[:, 1:2], sums[:, 0:1], -1.0 / (H * W), None,
                                        ALU.mult).then_inc(first_s, 1)
                for c in range(SLICES - 1):
                    dve.wait_ge(first_s, SLICES + 2 + 2 * c)
                    nc.vector.tensor_scalar(centered, first[:, 1, c].rearrange("p r w -> p (r w)"),
                                            neg_mean_c[:, 1:2], None, ALU.add).then_inc(first_s, 1)
                    dve.wait_ge(first_s, SLICES + 3 + 2 * c)
                    nc.vector.scalar_tensor_tensor(centered, centered, 1.0, centered, ALU.mult, ALU.mult,
                                                   accum_out=part_sq[:, 1, c:c + 1]).then_inc(first_s, 1)

            measure_first()
            dve.wait_ge(small_in, 32)
            nc.vector.reduce_sum(pb_f[:, :, DIRS], pb_f[:, :, 0:DIRS], axis=AX.X, negate=True).then_inc(pb_sum, 1)
            dve.wait_ge(first_s, SLICES + 2 + 2 * (SLICES - 1))
            dve.wait_ge(consts, CONSTS)
            group_stats(0)
            dve.wait_ge(weights_in, 16)
            nc.vector.tensor_copy(w_hi[:, :, w_dirs], w_raw[:, :, w_dirs]).then_inc(w_hi_s, 1)
            dve.sem_inc(prod_s, PROD0)
            for n in range(2):
                for j in range(NT):
                    for g in range(HALVES):
                        tap(n, n, g, j)

            def body(n0, b0, last):
                for nl in range(STEPS):
                    t, par, n = nl % TILES, nl // TILES, n0 + nl
                    for u in range(UNITS):
                        multiply(n0, b0 + par, nl, u)
                        if u < NT and not (last and nl + 2 >= STEPS):
                            for g in range(HALVES):
                                tap(n + 2, nl + 2, g, u)
                        if (t, u) == (3, STATS_AT) and not (last and par):
                            group_stats(b0 + par + 1)

            loop(dve, body)

        @block.tensor
        def _(pe):
            def make_maps(n0, nl, u):
                n, par, q = n0 + nl, nl % 2, nl * UNITS + u
                pe.wait_ge(prod_s, n0 * UNITS + (last_user(q) + 1 + PROD0))
                if u == 0:
                    pe.wait_ge(hhi_s, n + 1)
                if u == LAST:
                    pe.wait_ge(ninth_s, NINTH)
                for side in range(2):
                    d, g = unit_map(u, side)
                    col = d * C + g * P
                    steps = [(w, hhi, kk) for kk in range(HALVES) for w in (w_hi, w_lo)]
                    steps += [(w_hi, hlo, kk) for kk in range(HALVES)]
                    for s, (w, h, kk) in enumerate(steps):
                        if u == 0 and side == 0 and s == 2 * HALVES:
                            pe.wait_ge(hlo_s, n + 1)
                        last = nc.tensor.matmul(maps(q)[:, side, :], w[:, kk, col:col + P], h[par][:, kk, :],
                                                start=s == 0, stop=s == len(steps) - 1)
                    last.then_inc(maps_s, 1)

            pe.wait_ge(w_lo_s, 1)

            def body(n0, b0, last):
                for nl in range(STEPS):
                    for u in range(UNITS):
                        make_maps(n0, nl, u)

            loop(pe, body)


def kernel(x, L0_conv_dw_weight, L0_conv_pw_weight, L0_conv_pw_bias):
    import numpy as np
    import concourse.bacc as bacc
    from concourse.bass_utils import run_bass_kernel_spmd

    x = np.ascontiguousarray(x)
    arrays = {
        "x": x,
        "pw_t": np.ascontiguousarray(np.asarray(L0_conv_pw_weight).T),
        "pw_b": np.ascontiguousarray(np.asarray(L0_conv_pw_bias).reshape(8, -1, 128).transpose(2, 1, 0)),
        "dw": np.ascontiguousarray(L0_conv_dw_weight).reshape(x.shape[1], 9),
    }
    nc = bacc.Bacc("TRN2", target_bir_lowering=False, num_devices=1)
    args = {k: nc.dram_tensor(k, a.shape, mybir.dt.from_np(a.dtype), kind="ExternalInput").ap()
            for k, a in arrays.items()}
    out = nc.dram_tensor("out", x.shape, mybir.dt.float32, kind="ExternalOutput").ap()
    preact_directional_conv(nc, out=out, **args)
    r = run_bass_kernel_spmd(nc, [arrays], core_ids=[0])
    return r.results[0]["out"]
```
